# Optimizing a Trainium2 kernel written in Bass

```python
import numpy as np
import jax
import jax.numpy as jnp

def _softmax(x, axis=-1):
    return jax.nn.softmax(x, axis=axis)

def _gelu(x):
    return jax.nn.gelu(x, approximate=True)

def _silu(x):
    return jax.nn.silu(x)

def _sigmoid(x):
    return jax.nn.sigmoid(x)

def _layernorm(x, axis=-1, eps=1e-05):
    m = jnp.mean(x, axis=axis, keepdims=True)
    v = jnp.var(x, axis=axis, keepdims=True)
    return (x - m) / jnp.sqrt(v + eps)

def _scatter_add(tgt, idx, src, axis=0):
    return tgt.at[idx].add(src)

def _segment_sum(src, seg, n):
    return jax.ops.segment_sum(src, seg, n)
kernel_name = 'mk_seq_postln_d1_jaxref_r4_d9430c'

def setup_inputs(seed: int=0):
    np.random.seed(seed)
    _w = jnp.asarray

    def _L0_attn_setup():
        import jax, jax.numpy as jnp
        import numpy as np
        H = 1024
        D = 2048
        N = 16
        K = 4
        R = 64
        BATCH = 1
        L = 512
        EPS = 1e-06

        def _rmsnorm(x, w):
            return x * jax.lax.rsqrt(jnp.mean(x * x, axis=-1, keepdims=True) + EPS) * w
        key = jax.random.key(seed)
        ks = jax.random.split(key, 10)
        s = 0.02
        return {'hidden_states': jax.random.normal(ks[0], (BATCH, L, H), jnp.float32), 'W_in': jax.random.normal(ks[1], (2 * D, H), jnp.float32) * s, 'conv_w': jax.random.normal(ks[2], (D, K), jnp.float32) * s, 'conv_b': jax.random.normal(ks[3], (D,), jnp.float32) * s, 'Wx': jax.random.normal(ks[4], (R + 2 * N, D), jnp.float32) * s, 'dt_ln_w': jnp.ones((R,), jnp.float32), 'b_ln_w': jnp.ones((N,), jnp.float32), 'c_ln_w': jnp.ones((N,), jnp.float32), 'Wdt': jax.random.normal(ks[5], (D, R), jnp.float32) * s, 'dt_bias': jax.random.normal(ks[6], (D,), jnp.float32) * s, 'A': -jnp.exp(jax.random.normal(ks[7], (D, N), jnp.float32) * 0.5), 'D_param': jnp.ones((D,), jnp.float32), 'W_out': jax.random.normal(ks[8], (H, D), jnp.float32) * s}
    _L0_attn_in = _L0_attn_setup()

    def _L0_ffn_setup():
        import jax, jax.numpy as jnp
        import numpy as np
        RANKS = (8, 16, 32, 64)
        TOPK = 1
        SCALING = 1.0 / 4
        key = jax.random.key(seed)
        ks = jax.random.split(key, 7)
        D_IN, D_OUT, MAX_R, N_RANKS = (1024, 1024, 64, len(RANKS))
        B_, S_ = (4, 512)
        return {'hidden_states': jax.random.normal(ks[0], (B_, S_, D_IN), jnp.float32), 'W': jax.random.normal(ks[1], (D_OUT, D_IN), jnp.float32) * 0.02, 'b': jax.random.normal(ks[2], (D_OUT,), jnp.float32) * 0.02, 'A': jax.random.normal(ks[3], (MAX_R, D_IN), jnp.float32) * 0.02, 'B': jnp.zeros((D_OUT, MAX_R), jnp.float32) + jax.random.normal(ks[4], (D_OUT, MAX_R), jnp.float32) * 0.02, 'gate_w': jax.random.normal(ks[5], (N_RANKS, D_IN), jnp.float32) * 0.02, 'gate_b': jax.random.normal(ks[6], (N_RANKS,), jnp.float32) * 0.02}
    _L0_ffn_in = _L0_ffn_setup()
    _d = {'L0_attn_hidden_states': _L0_attn_in['hidden_states'], 'L0_attn_W_in': _L0_attn_in['W_in'], 'L0_attn_conv_w': _L0_attn_in['conv_w'], 'L0_attn_conv_b': _L0_attn_in['conv_b'], 'L0_attn_Wx': _L0_attn_in['Wx'], 'L0_attn_dt_ln_w': _L0_attn_in['dt_ln_w'], 'L0_attn_b_ln_w': _L0_attn_in['b_ln_w'], 'L0_attn_c_ln_w': _L0_attn_in['c_ln_w'], 'L0_attn_Wdt': _L0_attn_in['Wdt'], 'L0_attn_dt_bias': _L0_attn_in['dt_bias'], 'L0_attn_A': _L0_attn_in['A'], 'L0_attn_D_param': _L0_attn_in['D_param'], 'L0_attn_W_out': _L0_attn_in['W_out'], 'L0_ffn_W': _L0_ffn_in['W'], 'L0_ffn_b': _L0_ffn_in['b'], 'L0_ffn_A': _L0_ffn_in['A'], 'L0_ffn_B': _L0_ffn_in['B'], 'L0_ffn_gate_w': _L0_ffn_in['gate_w'], 'L0_ffn_gate_b': _L0_ffn_in['gate_b']}
    _x0 = _d['L0_attn_hidden_states']
    _d['L0_attn_hidden_states'] = jax.random.normal(jax.random.fold_in(jax.random.key(seed), 1), (4, 512, 1024), dtype=_x0.dtype)
    del _x0
    return _d

def reference(L0_attn_hidden_states, L0_attn_W_in, L0_attn_conv_w, L0_attn_conv_b, L0_attn_Wx, L0_attn_dt_ln_w, L0_attn_b_ln_w, L0_attn_c_ln_w, L0_attn_Wdt, L0_attn_dt_bias, L0_attn_A, L0_attn_D_param, L0_attn_W_out, L0_ffn_W, L0_ffn_b, L0_ffn_A, L0_ffn_B, L0_ffn_gate_w, L0_ffn_gate_b):

    def _L0_attn_ref(hidden_states, W_in, conv_w, conv_b, Wx, dt_ln_w, b_ln_w, c_ln_w, Wdt, dt_bias, A, D_param, W_out):
        import jax, jax.numpy as jnp
        import numpy as np
        H = 1024
        D = 2048
        N = 16
        K = 4
        R = 64
        BATCH = 1
        L = 512
        EPS = 1e-06

        def _rmsnorm(x, w):
            return x * jax.lax.rsqrt(jnp.mean(x * x, axis=-1, keepdims=True) + EPS) * w
        proj = hidden_states @ W_in.T
        u, gate = jnp.split(proj, 2, axis=-1)
        x = jnp.transpose(u, (0, 2, 1))
        x = jax.lax.conv_general_dilated(x, conv_w[:, None, :], window_strides=(1,), padding=[(K - 1, 0)], dimension_numbers=('NCH', 'OIH', 'NCH'), feature_group_count=D)
        u = jax.nn.silu(jnp.transpose(x, (0, 2, 1)) + conv_b)
        ssm_p = u @ Wx.T
        dt, Bm, Cm = jnp.split(ssm_p, [R, R + N], axis=-1)
        dt = _rmsnorm(dt, dt_ln_w)
        Bm = _rmsnorm(Bm, b_ln_w)
        Cm = _rmsnorm(Cm, c_ln_w)
        delta = jax.nn.softplus(dt @ Wdt.T + dt_bias)

        def step(state, xs):
            d_t, B_t, C_t, u_t = xs
            dA = jnp.exp(d_t[..., None] * A)
            state = dA * state + (d_t * u_t)[..., None] * B_t[:, None, :]
            y_t = jnp.einsum('bdn,bn->bd', state, C_t)
            return (state, y_t)
        init = jnp.zeros((hidden_states.shape[0], D, N), hidden_states.dtype)
        xs = (jnp.swapaxes(delta, 0, 1), jnp.swapaxes(Bm, 0, 1), jnp.swapaxes(Cm, 0, 1), jnp.swapaxes(u, 0, 1))
        _, ys = jax.lax.scan(step, init, xs)
        y = jnp.swapaxes(ys, 0, 1) + u * D_param
        y = y * jax.nn.silu(gate)
        return y @ W_out.T

    def _L0_ffn_ref(hidden_states, W, b, A, B, gate_w, gate_b):
        import jax, jax.numpy as jnp
        import numpy as np
        RANKS = (8, 16, 32, 64)
        TOPK = 1
        SCALING = 1.0 / 4
        bsz, seq, d_in = hidden_states.shape
        out = jnp.einsum('bsd,od->bso', hidden_states, W) + b
        x = hidden_states.reshape(-1, d_in)
        scores = x @ gate_w.T + gate_b
        probs = jax.nn.softmax(scores, axis=-1)
        routing_weights, selected = jax.lax.top_k(probs, TOPK)
        routing_weights = routing_weights / jnp.sum(routing_weights, axis=-1, keepdims=True)
        lora_outputs = jnp.stack([x @ A[:r, :].T @ B[:, :r].T for r in RANKS], axis=1)
        sel = jnp.take_along_axis(lora_outputs, selected[:, :, None], axis=1)
        final = jnp.sum(sel * routing_weights[:, :, None], axis=1)
        return out + final.reshape(bsz, seq, -1)
    x = L0_attn_hidden_states
    x = _layernorm(x + _L0_attn_ref(x, L0_attn_W_in, L0_attn_conv_w, L0_attn_conv_b, L0_attn_Wx, L0_attn_dt_ln_w, L0_attn_b_ln_w, L0_attn_c_ln_w, L0_attn_Wdt, L0_attn_dt_bias, L0_attn_A, L0_attn_D_param, L0_attn_W_out), axis=-1)
    x = _layernorm(x + _L0_ffn_ref(x, L0_ffn_W, L0_ffn_b, L0_ffn_A, L0_ffn_B, L0_ffn_gate_w, L0_ffn_gate_b), axis=-1)
    return x

_drawn_inputs = setup_inputs


def setup_inputs(seed=0):
    import zlib

    import numpy as np

    out = dict(_drawn_inputs(seed))
    spreads = {'L0_attn_dt_ln_w': (1.0, 0.6),
     'L0_attn_b_ln_w': (1.0, 0.6),
     'L0_attn_c_ln_w': (1.0, 0.6),
     'L0_attn_D_param': (1.0, 0.6)}
    factors = {'L0_attn_conv_b': 3.197,
     'L0_attn_Wdt': 8.0,
     'L0_attn_dt_bias': 46.311,
     'L0_attn_A': 64.0,
     'L0_ffn_b': 3.513,
     'L0_ffn_gate_b': 25.106}
    for name, (base, spread) in spreads.items():
        noise = np.random.default_rng([zlib.crc32(name.encode()), seed]).standard_normal(out[name].shape)
        drawn = base * np.exp(spread * noise) if base else spread * noise
        out[name] = jnp.asarray(drawn.astype(out[name].dtype))
    for name, factor in factors.items():
        out[name] = (out[name] * factor).astype(out[name].dtype)
    return out
```

```python
from contextlib import ExitStack

import concourse.bass as bass
from concourse import mybir

F32 = mybir.dt.float32
ALU = mybir.AluOpType
ACT = mybir.ActivationFunctionType
AX = mybir.AxisListType

P = 128
MIXER_EPS = 1e-6
LN_EPS = 1e-5
LORA_RANKS = (8, 16, 32, 64)
SOFTPLUS_CAP = 30.0


class Lane:

    def __init__(self, semaphore):
        self.semaphore, self.count, self.queue = semaphore, 0, []

    def op(self, build, *waits, signal=True):
        self.queue.append((build, [w for w in waits if w is not None], self.semaphore if signal else None, 1))
        self.count += signal
        return (self.semaphore, self.count)

    def dma(self, build, done, *waits):
        self.queue.append((build, [w for w in waits if w is not None], done.semaphore, 16))
        done.count += 16
        return (done.semaphore, done.count)

    def wait(self, *waits):
        self.queue.append((None, list(waits), None, 0))

    def play(self, engine):
        reached = {}
        for build, waits, semaphore, step in self.queue:
            for sem, value in waits:
                if reached.get(id(sem), 0) < value:
                    engine.wait_ge(sem, value)
                    reached[id(sem)] = value
            if build is not None:
                ins = build(engine)
                if semaphore is not None:
                    ins.then_inc(semaphore, step)


class DmaCounter:
    def __init__(self, semaphore):
        self.semaphore, self.count = semaphore, 0


class Ring:

    def __init__(self, buffers, settle=None):
        self.buffers, self.next, self.settle = buffers, 0, settle
        self.free = [()] * len(buffers)

    def take(self):
        i = self.next % len(self.buffers)
        self.next += 1
        while self.free[i] is None:
            self.settle()
        marks, self.free[i] = self.free[i], None
        return i, self.buffers[i], marks

    def release(self, i, *marks):
        self.free[i] = marks


TAIL = "tail"


class Background:

    def __init__(self):
        self.tasks, self.head, self.tails, self.owed = [], None, [], 0.0

    def add(self, task, after_all=False):
        self.tasks.append((task, after_all))

    def run(self, amount):
        self.owed += amount
        while self.owed > 0 and (self.head is not None or self.tasks):
            if self.head is None:
                task, after_all = self.tasks.pop(0)
                while after_all and self.tails:
                    self.step_tails()
                self.head = task()
            try:
                cost = next(self.head)
            except StopIteration:
                self.head = None
                continue
            if cost is TAIL:
                self.tails.append(self.head)
                self.head = None
            else:
                self.owed -= cost
        if self.head is None and not self.tasks:
            self.owed = 0.0

    def add_beside(self, task):
        while next(task) is not TAIL:
            pass
        self.tails.append(task)

    def step_tails(self):
        for tail in list(self.tails):
            if not tail.gi_running and next(tail, None) is None and tail in self.tails:
                self.tails.remove(tail)

    def drain(self, step):
        while self.head is not None or self.tasks or self.tails:
            self.run(step)
            self.step_tails()


def build_mixer_ffn(nc, ins, out):
    x_rows, x_cols = ins["x_rows"], ins["x_cols"]
    NSEQ, T, H = x_rows.shape
    N = ins["A"].shape[2]
    R = ins["dt_ln_w"].shape[0]
    D = ins["A"].shape[1] * P
    TT, HT, DT = T // P, H // P, D // P
    GT = 4
    NG = DT // GT
    S = R + 2 * N
    KC = ins["conv_w"].shape[2]
    NR = len(LORA_RANKS)
    RMAX = LORA_RANKS[-1]
    WK = 8
    assert T == 512 and H == WK * P and R == RMAX == 64 and 2 * R == P and D == 2 * H

    with ExitStack() as ctx:
        def sbuf(name, shape):
            return ctx.enter_context(nc.sbuf_tensor(name, shape, F32))

        def psum(name, shape):
            return ctx.enter_context(nc.psum_tensor(name, shape, F32))

        def sem(name):
            return ctx.enter_context(nc.semaphore(name))

        b_rows_dram = nc.dram_tensor("b_rows", [NSEQ, N, T], F32, kind="Internal").ap()

        token_bufs = [sbuf(f"token_buf{i}", [P, HT * T]) for i in range(3)]
        background = Background()
        settle = background.step_tails
        w_slots = Ring([sbuf(f"w_slot{i}", [P, WK * P]) for i in range(4)])
        chan = [sbuf(f"channels{i}", [P, DT, T]) for i in range(2)]
        delta = sbuf("delta", [P, 2, GT, T])
        du = sbuf("delta_u", [P, GT, T])
        b_bcast = Ring([sbuf(f"b_bcast{i}", [P, T]) for i in range(3)])
        drive = Ring([sbuf(f"drive{i}", [P, GT, T]) for i in range(2)])
        decay = Ring([sbuf(f"decay{i}", [P, T]) for i in range(4)])
        y_acc = sbuf("y_acc", [P, TT, GT * P])
        scratch = Ring([sbuf(f"scratch{i}", [P, T]) for i in range(6)], settle)
        identity = sbuf("identity", [P, P])
        a_sb = sbuf("a_sb", [P, DT, N])
        conv_w = sbuf("conv_w_sb", [P, DT, KC])
        conv_b = sbuf("conv_b_sb", [P, DT])
        dt_bias = sbuf("dt_bias_sb", [P, DT])
        d_param = sbuf("d_param_sb", [P, DT])
        wdt = sbuf("wdt_sb", [P, DT // 2 * P])
        dt_ln_w = sbuf("dt_ln_w_sb", [P, 1])
        b_ln_w = sbuf("b_ln_w_sb", [N, 1])
        c_ln_w = sbuf("c_ln_w_sb", [P, N])
        ffn_b = sbuf("ffn_b_sb", [P, HT])
        gate_b = sbuf("gate_b_sb", [P, NR])
        lora_b = sbuf("lora_b_sb", [P, HT // 2 * P])
        ssm = sbuf("ssm", [P, TT, S])
        ssm_rstd = sbuf("ssm_rstd", [P, 3, TT])
        dt_rows = sbuf("dt_rows", [P, TT, 2 * R])
        c_rows = [sbuf(f"c_rows{i}", [P, TT, N]) for i in range(2)]
        dt_cols = sbuf("dt_cols", [P, T])
        b_cols = sbuf("b_cols", [N, T])
        ln_stats = sbuf("ln_stats", [P, TT, H // 512, 6])
        ln_mv = sbuf("ln_mv", [P, TT, 2])
        ln_rstd = sbuf("ln_rstd", [P, TT])
        score = sbuf("score", [P, TT, NR])
        prob = sbuf("prob", [P, TT, NR])
        keep = sbuf("keep", [P, TT, NR])
        row_stat = sbuf("row_stat", [P, 2, TT])
        lora_rows = sbuf("lora_rows", [P, TT, 2 * RMAX])
        lora_cols = sbuf("lora_cols", [P, T])
        lora_raw = sbuf("lora_raw", [P, TT, RMAX + NR])

        product_banks = Ring([psum(f"product{i}", [P, T]) for i in range(2)], settle)
        state_banks = [psum(f"state_t{i}", [P, GT * P]) for i in range(TT)]
        side_banks = Ring([psum(f"side{i}", [P, T]) for i in range(2)], settle)

        pe, dve, act, pool, sp = (Lane(sem(n)) for n in
                                  ("tensor_done", "vector_done", "scalar_done", "pool_done", "sync_done"))
        const_loaded = DmaCounter(sem("const_loaded"))
        w_loaded = [DmaCounter(sem(f"w_loaded{i}")) for i in range(len(w_slots.buffers))]
        token_loaded = [DmaCounter(sem(f"token_loaded{i}")) for i in range(3)]
        b_loaded = [DmaCounter(sem(f"b_loaded{i}")) for i in range(len(b_bcast.buffers))]
        b_stored = DmaCounter(sem("b_stored"))
        out_stored = DmaCounter(sem("out_stored"))

        w_plan, w_ready = [], []

        def prefetch():
            while w_plan and w_slots.free[w_slots.next % len(w_slots.buffers)] is not None:
                parts, cols = w_plan.pop(0)
                i, slot, free = w_slots.take()
                tile = slot[:, 0:WK * cols].rearrange("p (k m) -> p k m", k=WK)
                for a, z, src in parts:
                    mark = sp.dma(lambda e, dst=tile[:, :, a:z], src=src: e.dma_start(dst, src), w_loaded[i], *free)
                w_ready.append((i, tile, mark))

        def release_w(i, mark):
            w_slots.release(i, mark)
            prefetch()

        def plan_product(name, *index):
            w_plan.append(([(0, P, ins[name][index])], P))

        token_free = [(), (), ()]
        ROWS = 2

        def load_tokens(i, src, view):
            dst = token_bufs[i][:, :].rearrange(*view[:1], **view[1])
            return dst, sp.dma(lambda e: e.dma_start(dst, src), token_loaded[i], *token_free[i])

        x_tiles = {}

        def load_x(b):
            x_tiles[b] = load_tokens(b % 2, x_cols[b], ("p (k t) -> p k t", dict(k=HT)))

        MM_COST = 0.86
        TURN_COST = 0.06

        def product(moving, n_k, *waits, extra=None):
            bi, bank, free = product_banks.take()
            for k in range(n_k):
                if k % WK == 0:
                    w_i, w, loaded = w_ready.pop(0)
                last = k == n_k - 1 and extra is None
                end_of_slot = k % WK == WK - 1
                mark = pe.op(lambda e, w=w, k=k, last=last: e.matmul(
                    bank[:, :], w[:, k % WK, :], moving(k), start=(k == 0), stop=last),
                    loaded, *(free + waits if k == 0 else ()), signal=last or end_of_slot)
                if end_of_slot:
                    release_w(w_i, mark)
                if k % 4 == 3:
                    yield 4 * MM_COST
            if extra is not None:
                lhsT, rhs, extra_mark = extra
                mark = pe.op(lambda e: e.matmul(bank[:, :], lhsT, rhs, start=False, stop=True), extra_mark)
                yield MM_COST
            return bi, bank, mark

        def turn(bank, tiles, *waits):
            for i, tile in enumerate(tiles):
                mark = pe.op(lambda e, i=i, tile=tile: e.transpose(
                    bank[0:tile.shape[1], i * P:(i + 1) * P], tile, identity[:, :]), *waits,
                    signal=(i == len(tiles) - 1))
            return mark

        u_ready = {}
        chan_free = [(), ()]

        def make_u(b, j):
            x_tile, x_mark = x_tiles[b]
            bi, bank, mark = yield from product(lambda k: x_tile[:, k, :], HT, x_mark)
            yield TAIL
            ci, conv, conv_free = scratch.take()
            done = act.op(lambda e: e.activation(conv[:, :], bank[:, :], ACT.Identity, bias=conv_b[:, j:j + 1],
                                                 scale=conv_w[:, j, KC - 1:KC]), mark, taps_halved, *conv_free)
            for back in range(1, KC):
                done = dve.op(lambda e, back=back: e.scalar_tensor_tensor(
                    conv[:, back:T], bank[:, 0:T - back], conv_w[:, j, KC - 1 - back:KC - back],
                    conv[:, back:T], ALU.mult, ALU.add), done, mark)
            product_banks.release(bi, done)
            yield 0
            ti, th, th_free = scratch.take()
            tanh = act.op(lambda e: e.activation(th[:, :], conv[:, :], ACT.Tanh), done, *th_free)
            yield 0
            u = chan[b % 2][:, j, :]
            made = dve.op(lambda e: e.scalar_tensor_tensor(u, th[:, :], 1.0, conv[:, :], ALU.add, ALU.mult),
                          tanh, *chan_free[b % 2])
            scratch.release(ci, made)
            scratch.release(ti, made)
            u_ready[b, j] = made

        phase = {}
        free_after = dict(c_rows=[(), ()], ssm=(), dt_rows=(), dt_cols=(), b_cols=(), lora_rows=(), lora_cols=(),
                          du=(), ln=())

        def plan_ssm():
            for half in range(2):
                w_plan.append(([(0, S, ins["w_x"][:, half * WK:(half + 1) * WK, :])], S))

        def make_ssm(b):
            u = chan[b % 2]
            halves = [w_ready.pop(0), w_ready.pop(0)]
            si, bank, free = side_banks.take()
            rows = bank[:, 0:TT * S].rearrange("p (a s) -> p a s", a=TT)
            for tt in range(TT):
                for k in range(DT):
                    _, w, loaded = halves[k // WK]
                    mark = pe.op(lambda e, tt=tt, k=k, w=w: e.matmul(
                        rows[:, tt, :], u[:, k, tt * P:(tt + 1) * P], w[:, k % WK, :],
                        start=(k == 0), stop=(k == DT - 1)), loaded, u_ready[b, k], *free,
                        signal=(k == DT - 1))
                yield DT * 0.17
            for w_i, _, _ in halves:
                release_w(w_i, mark)
            yield TAIL
            copied = act.op(lambda e: e.activation(ssm[:, :, :], rows, ACT.Copy), mark, *free_after["ssm"])
            side_banks.release(si, copied)
            yield 0
            squares = lora_rows[:, :, 0:S]
            squared = dve.op(lambda e: e.tensor_tensor(squares, ssm[:, :, :], ssm[:, :, :], ALU.mult),
                             copied, *free_after["lora_rows"])
            segments = ((0, R), (R, R + N), (R + N, S))
            for i, (a, z) in enumerate(segments):
                summed = dve.op(lambda e, i=i, a=a, z=z: e.tensor_reduce(
                    ssm_rstd[:, i, :], squares[:, :, a:z], AX.X, ALU.add), squared)
            free_after["lora_rows"] = (summed,)
            for i, (a, z) in enumerate(segments):
                means = dve.op(lambda e, i=i, a=a, z=z: e.tensor_scalar(
                    ssm_rstd[:, i, :], ssm_rstd[:, i, :], 1.0 / (z - a), MIXER_EPS, ALU.mult, ALU.add), summed)
            rooted = act.op(lambda e: e.activation(ssm_rstd[:, :, :], ssm_rstd[:, :, :], ACT.Sqrt), means)
            yield 0
            rstd = dve.op(lambda e: e.reciprocal(ssm_rstd[:, :, :], ssm_rstd[:, :, :]), rooted)
            c = c_rows[b % 2]
            for tt in range(TT):
                for half in range(2):
                    dt_done = dve.op(lambda e, tt=tt, half=half: e.tensor_scalar(
                        dt_rows[:, tt, half * R:(half + 1) * R], ssm[:, tt, 0:R], ssm_rstd[:, 0, tt:tt + 1], None,
                        ALU.mult), rstd, *free_after["dt_rows"])
                b_done = dve.op(lambda e, tt=tt: e.tensor_scalar(
                    ssm[:, tt, R:R + N], ssm[:, tt, R:R + N], ssm_rstd[:, 1, tt:tt + 1], None, ALU.mult), rstd)
                c_done = dve.op(lambda e, tt=tt: e.scalar_tensor_tensor(
                    c[:, tt, :], ssm[:, tt, R + N:S], ssm_rstd[:, 2, tt:tt + 1], c_ln_w[:, :], ALU.mult, ALU.mult),
                    rstd, *free_after["c_rows"][b % 2])
            yield 0
            si, bank, free = side_banks.take()
            mark = turn(bank, [dt_rows[:, tt, :] for tt in range(TT)], dt_done, *free)
            free_after["dt_rows"] = (mark,)
            dt_mark = act.op(lambda e, bank=bank: e.activation(dt_cols[:, :], bank[:, :], ACT.Copy, scale=dt_ln_w[:, :]),
                             mark, *free_after["dt_cols"])
            side_banks.release(si, dt_mark)
            si, bank, free = side_banks.take()
            mark = turn(bank, [ssm[:, tt, R:R + N] for tt in range(TT)], b_done, *free)
            free_after["ssm"] = (mark, c_done)
            b_mark = act.op(lambda e, bank=bank: e.activation(b_cols[:, :], bank[0:N, :], ACT.Copy, scale=b_ln_w[:, :]),
                            mark, *free_after["b_cols"])
            side_banks.release(si, b_mark)
            stored = sp.dma(lambda e: e.dma_start(b_rows_dram[b, :, :], b_cols[:, :]), b_stored, b_mark)
            free_after["b_cols"] = (stored,)
            phase[b] = dict(dt=dt_mark, b=stored, c=c_done)

        delta_free = {}
        delta_ready, du_ready = {}, {}

        def make_delta(b, g, t):
            j = g * GT + t
            half, col = j // (DT // 2), j % (DT // 2) * P
            dst = delta[:, g % 2, t, :]
            si, bank, free = side_banks.take()
            mark = pe.op(lambda e: e.matmul(
                bank[:, :], wdt[half * R:(half + 1) * R, col:col + P], dt_cols[half * R:(half + 1) * R, :],
                start=True, stop=True), phase[b]["dt"], *free)
            free_after["dt_cols"] = (mark,)
            yield MM_COST
            yield TAIL
            v = act.op(lambda e: e.activation(dst, bank[:, :], ACT.Identity, bias=dt_bias[:, j:j + 1]),
                       mark, *delta_free.get((g % 2, t), ()))
            side_banks.release(si, v)
            ei, ex, ex_free = scratch.take()
            capped = dve.op(lambda e: e.tensor_scalar(ex[:, :], dst, SOFTPLUS_CAP, None, ALU.min), v, *ex_free)
            yield 0
            exped = act.op(lambda e: e.activation(ex[:, :], ex[:, :], ACT.Exp), capped)
            logged = act.op(lambda e: e.activation(ex[:, :], ex[:, :], ACT.Ln, bias=1.0), exped)
            yield 0
            made = dve.op(lambda e: e.tensor_tensor(dst, dst, ex[:, :], ALU.max), logged)
            scratch.release(ei, made)
            delta_ready[b, g, t] = made

        def make_du(b, g):
            for t in range(GT):
                j = g * GT + t
                du_ready[b, g] = pool.op(lambda e, t=t, j=j: e.tensor_tensor(
                    du[:, t, :], delta[:, g % 2, t, :], chan[b % 2][:, j, :], ALU.mult),
                    delta_ready[b, g, t], u_ready[b, j], *free_after["du"])

        y_ready = {}
        y_acc_free = [()]

        def turn_y(b, g):
            for t in range(GT):
                j = g * GT + t
                si, bank, free = side_banks.take()
                mark = turn(bank, [y_acc[:, tt, t * P:(t + 1) * P] for tt in range(TT)], *last_add, *free)
                u = chan[b % 2][:, j, :]
                y_ready[b, j] = dve.op(lambda e, bank=bank, u=u, j=j: e.scalar_tensor_tensor(
                    u, u, d_param[:, j:j + 1], bank[:, :], ALU.mult, ALU.add), mark, du_ready[b, g])
                side_banks.release(si, y_ready[b, j])
            y_acc_free[0] = (mark,)

        def make_gated_y(b, j):
            x_tile, x_mark = x_tiles[b]
            bi, bank, mark = yield from product(lambda k: x_tile[:, k, :], HT, x_mark)
            token_free[b % 2] = (mark,)
            yield TAIL
            gi, gate, free = scratch.take()
            tanh = act.op(lambda e: e.activation(gate[:, :], bank[:, :], ACT.Tanh, scale=0.5), mark, *free)
            yield 0
            twice = dve.op(lambda e: e.scalar_tensor_tensor(
                gate[:, :], gate[:, :], 1.0, bank[:, :], ALU.add, ALU.mult), tanh)
            product_banks.release(bi, twice)
            yield 0
            y = chan[b % 2][:, j, :]
            y_ready[b, j] = dve.op(lambda e: e.scalar_tensor_tensor(
                y, y, 0.5, gate[:, :], ALU.mult, ALU.mult), twice, y_ready[b, j])
            scratch.release(gi, y_ready[b, j])

        rows = token_bufs[ROWS][:, :].rearrange("p (a h) -> p a h", a=TT)
        mixed = {}

        def load_rows(b):
            _, mixed["rows"] = load_tokens(ROWS, ins["x_rows"][b].rearrange("(a p) h -> p a h", p=P),
                                           ("p (a h) -> p a h", dict(a=TT)))

        def add_to_rows(h, bi, bank, mark, bias):
            ci, cols, free = scratch.take()
            copied = act.op(lambda e: e.activation(cols[:, :], bank[:, :], ACT.Identity, bias=bias), mark, *free)
            product_banks.release(bi, copied)
            yield 0
            si, side, free = side_banks.take()
            turned = turn(side, [cols[:, tt * P:(tt + 1) * P] for tt in range(TT)], copied, *free)
            scratch.release(ci, turned)
            yield 0
            dst = rows[:, :, h * P:(h + 1) * P]
            added = dve.op(lambda e: e.tensor_tensor(dst, side[:, :].rearrange("p (a q) -> p a q", a=TT), dst, ALU.add),
                           turned, mixed["rows"])
            side_banks.release(si, added)
            mixed["added"] = added

        def make_out(b, h):
            y = chan[b % 2]
            info = yield from product(lambda k: y[:, k, :], DT, *[y_ready[b, j] for j in range(DT)])
            chan_free[b % 2] = (info[2],)
            yield TAIL
            yield from add_to_rows(h, *info, 0.0)

        def layer_norm():
            yield TAIL
            for tt in range(TT):
                for i in range(H // 512):
                    stats = dve.op(lambda e, tt=tt, i=i: e.bn_stats(
                        ln_stats[:, tt, i, :], rows[:, tt, i * 512:(i + 1) * 512]), mixed["added"], *free_after["ln"])
                aggr = dve.op(lambda e, tt=tt: e.bn_aggr(ln_mv[:, tt, :], ln_stats[:, tt, :, :]), stats)
                yield 0
            added = dve.op(lambda e: e.tensor_scalar(ln_rstd[:, :], ln_mv[:, :, 1], LN_EPS, None, ALU.add), aggr)
            rooted = act.op(lambda e: e.activation(ln_rstd[:, :], ln_rstd[:, :], ACT.Sqrt), added)
            yield 0
            rstd = dve.op(lambda e: e.reciprocal(ln_rstd[:, :], ln_rstd[:, :]), rooted)
            mixed["normed"] = []
            for tt in range(TT):
                mixed["normed"].append(dve.op(lambda e, tt=tt: e.tensor_scalar(
                    rows[:, tt, :], rows[:, tt, :], ln_mv[:, tt, 0:1], ln_rstd[:, tt:tt + 1],
                    ALU.subtract, ALU.mult), rstd))
                if tt % 2:
                    yield 0
            free_after["ln"] = (mixed["normed"][-1],)

        def x1_by_columns(b):
            x1 = token_bufs[b % 2][:, :].rearrange("p (k t) -> p k t", k=HT)
            mixed["x1"] = x1
            for h in range(HT):
                si, bank, free = side_banks.take()
                mark = turn(bank, [rows[:, tt, h * P:(h + 1) * P] for tt in range(TT)], *mixed["normed"], *free)
                mixed["x1_mark"] = act.op(lambda e, h=h, bank=bank: e.activation(x1[:, h, :], bank[:, :], ACT.Copy),
                                          mark, *token_free[b % 2])
                side_banks.release(si, mixed["x1_mark"])
                yield 4 * TURN_COST
            mixed["rows"] = mark

        def plan_route():
            w_plan.append(([(0, RMAX, ins["lora_a"]), (RMAX, RMAX + NR, ins["gate_w"])], RMAX + NR))

        def route():
            x1, x1_mark = mixed["x1"], mixed["x1_mark"]
            w_i, w, loaded = w_ready.pop(0)
            si, bank, free = side_banks.take()
            C = RMAX + NR
            both = bank[:, 0:TT * C].rearrange("p (a c) -> p a c", a=TT)
            for tt in range(TT):
                for k in range(HT):
                    mark = pe.op(lambda e, tt=tt, k=k: e.matmul(
                        both[:, tt, :], x1[:, k, tt * P:(tt + 1) * P], w[:, k, :], start=(k == 0), stop=(k == HT - 1)),
                        loaded, x1_mark, *free, signal=(k == HT - 1))
                yield 1.0
            release_w(w_i, mark)
            copied = act.op(lambda e: e.activation(lora_raw[:, :, :], both, ACT.Copy), mark, *free_after["lora_raw"])
            side_banks.release(si, copied)
            yield TAIL

            def per_token(ap):
                return ap.unsqueeze(2).broadcast_to([P, TT, NR])
            gate_bias = gate_b[:, :].unsqueeze(1).broadcast_to([P, TT, NR])
            top, total = row_stat[:, 0, :], row_stat[:, 1, :]
            c = dve.op(lambda e: e.tensor_tensor(score[:, :, :], lora_raw[:, :, RMAX:C], gate_bias, ALU.add),
                       copied, *free_after["lora_rows"])
            c = dve.op(lambda e: e.tensor_reduce(top, score[:, :, :], AX.X, ALU.max), c)
            c = dve.op(lambda e: e.tensor_tensor(score[:, :, :], score[:, :, :], per_token(top), ALU.subtract), c)
            exped = act.op(lambda e: e.activation(prob[:, :, :], score[:, :, :], ACT.Exp), c)
            yield 0
            c = dve.op(lambda e: e.tensor_reduce(total, prob[:, :, :], AX.X, ALU.add), exped)
            c = dve.op(lambda e: e.reciprocal(total, total), c)
            c = dve.op(lambda e: e.tensor_tensor(prob[:, :, :], prob[:, :, :], per_token(total), ALU.mult), c)
            c = dve.op(lambda e: e.tensor_reduce(top, prob[:, :, :], AX.X, ALU.max), c)
            c = dve.op(lambda e: e.reciprocal(total, top), c)
            c = dve.op(lambda e: e.tensor_tensor(keep[:, :, 0], top, total, ALU.mult), c)
            c = dve.op(lambda e: e.tensor_tensor(score[:, :, :], prob[:, :, :], per_token(top), ALU.is_lt), c)
            for r in range(1, NR):
                c = dve.op(lambda e, r=r: e.tensor_tensor(
                    keep[:, :, r], keep[:, :, r - 1], score[:, :, r - 1], ALU.mult), c)
            yield 0
            start = 0
            for r, rank in enumerate(LORA_RANKS):
                for half in range(2):
                    dst = lora_rows[:, :, half * RMAX + start:half * RMAX + rank]
                    weight = keep[:, :, r:r + 1].broadcast_to([P, TT, rank - start])
                    masked = dve.op(lambda e, dst=dst, weight=weight, a=start, z=rank: e.tensor_tensor(
                        dst, lora_raw[:, :, a:z], weight, ALU.mult), c, *free_after["lora_rows"])
                start = rank
            free_after["lora_raw"] = (masked,)
            yield 0
            si, bank2, free = side_banks.take()
            mark = turn(bank2, [lora_rows[:, tt, :] for tt in range(TT)], masked, *free)
            free_after["lora_rows"] = (mark,)
            mixed["lora"] = act.op(lambda e: e.activation(lora_cols[:, :], bank2[:, :], ACT.Copy), mark,
                                   *free_after["lora_cols"])
            side_banks.release(si, mixed["lora"])

        free_after["lora_raw"] = ()

        def make_ffn(b, h):
            x1 = mixed["x1"]
            half, col = h // (HT // 2), h % (HT // 2) * P
            low_rank = lambda: (lora_b[half * RMAX:(half + 1) * RMAX, col:col + P],
                                lora_cols[half * RMAX:(half + 1) * RMAX, :], mixed["lora"])
            info = yield from product(lambda k: x1[:, k, :], HT, mixed["x1_mark"], extra=low_rank())
            free_after["lora_cols"] = token_free[b % 2] = (info[2],)
            yield TAIL
            yield from add_to_rows(h, *info, ffn_b[:, h:h + 1])

        def store_rows(b):
            token_free[ROWS] = (sp.dma(lambda e: e.dma_start(out[b].rearrange("(a p) h -> p a h", p=P), rows),
                                       out_stored, *mixed["normed"]),)
            yield 0

        state_bank_free = [() for _ in range(TT)]
        drive_of, decay_of, turned_of, scanned_of, b_of = {}, {}, {}, {}, {}
        last_add = [None] * TT
        units = [(b, g, n) for b in range(NSEQ) for g in range(NG) for n in range(N)]

        def fetch_b(unit):
            b, g, n = unit
            i, tile, free = b_bcast.take()
            b_of[unit] = (i, tile, sp.dma(lambda e: e.dma_start(
                tile[:, :], b_rows_dram[b, n, :].partition_broadcast(P)), b_loaded[i], phase[b]["b"], *free))

        def make_drive(unit):
            b, g, n = unit
            i, tile, loaded = b_of.pop(unit)
            di, dst, free = drive.take()
            row = tile[:, :].unsqueeze(1).broadcast_to([P, GT, T])
            made = pool.op(lambda e: e.tensor_tensor(dst[:, :, :], du[:, :, :], row, ALU.mult),
                           loaded, du_ready[b, g], *free)
            b_bcast.release(i, made)
            free_after["du"] = (made,)
            drive_of[unit] = (di, dst, made)

        def make_decay(unit, t):
            b, g, n = unit
            j = g * GT + t
            i, dst, free = decay.take()
            made = act.op(lambda e: e.activation(dst[:, :], delta[:, g % 2, t, :], ACT.Exp, scale=a_sb[:, j, n:n + 1]),
                          delta_ready[b, g, t], *free)
            delta_free[g % 2, t] = (made,)
            decay_of[unit, t] = (i, dst, made)

        def scan(unit, t):
            _, state, driven = drive_of[unit]
            i, dec, decayed = decay_of.pop((unit, t))
            done = dve.op(lambda e: e.tensor_tensor_scan(
                state[:, t, :], dec[:, :], state[:, t, :], 0.0, ALU.mult, ALU.add), driven, decayed)
            decay.release(i, done)
            scanned_of[unit, t] = done

        def turn_state(unit):
            di, state, _ = drive_of.pop(unit)
            for tt in range(TT):
                turned_of[unit, tt] = turn(state_banks[tt], [state[:, t, tt * P:(tt + 1) * P] for t in range(GT)],
                                           scanned_of[unit, GT - 1], *state_bank_free[tt])
            drive.release(di, turned_of[unit, TT - 1])

        def add_y(unit, tt):
            b, g, n = unit
            c = c_rows[b % 2][:, tt, n:n + 1]
            mark = turned_of.pop((unit, tt))
            if n == 0:
                done = dve.op(lambda e: e.tensor_scalar(y_acc[:, tt, :], state_banks[tt][:, :], c, None, ALU.mult),
                              mark, phase[b]["c"], *y_acc_free[0])
            else:
                done = dve.op(lambda e: e.scalar_tensor_tensor(
                    y_acc[:, tt, :], state_banks[tt][:, :], c, y_acc[:, tt, :], ALU.mult, ALU.add),
                    mark, last_add[tt])
            last_add[tt] = done
            state_bank_free[tt] = (done,)
            free_after["c_rows"][b % 2] = (done,)

        def add_tasks(b):
            cost = [0.0]

            def add(task, us, after_all=False):
                background.add(task, after_all)
                cost[0] += us

            def add_u(tiles):
                if b + 1 < NSEQ:
                    for j in tiles:
                        plan_product("w_in", j)
                        add(lambda j=j: make_u(b + 1, j), HT * MM_COST)

            def add_gates(s, g):
                if 0 <= s < NSEQ:
                    for j in range(g * GT, (g + 1) * GT):
                        plan_product("w_in", DT + j)
                        add(lambda j=j: make_gated_y(s, j), HT * MM_COST)

            def call(function, *args):
                function(*args)
                yield 0

            mix = 0 <= b - 1
            add_gates(b - 1, NG - 1)
            if mix:
                s = b - 1
                add(lambda: call(load_rows, s), 0, after_all=True)
                for h in range(HT):
                    plan_product("w_out", h, 0)
                    plan_product("w_out", h, 1)
                    add(lambda h=h: make_out(s, h), DT * MM_COST)
                add(layer_norm, 0, after_all=True)
            else:
                if b == 0:
                    add(lambda: call(load_x, 1), 0)
                add_u(range(0, DT // 2))
            if b < NSEQ and b >= 0:
                add_gates(b, 0)
            if mix:
                add(lambda: x1_by_columns(s), 2.0, after_all=True)
                plan_route()
                add(route, 4.0)
            if mix:
                for h in range(HT):
                    plan_product("w_ffn", h)
                    add(lambda h=h: make_ffn(s, h), (HT + 1) * MM_COST, after_all=(h == 0))
                add(layer_norm, 0, after_all=True)
            else:
                add_u(range(DT // 2, DT * 3 // 4))
            if b < NSEQ:
                add_gates(b, 1)
            if mix:
                add(lambda: store_rows(s), 0, after_all=True)
            if b + 1 < NSEQ:
                if mix:
                    add(lambda: call(load_x, b + 1), 0)
                add_u(range(0 if mix else DT * 3 // 4, DT))
                plan_ssm()
                add(lambda: make_ssm(b + 1), 11.0, after_all=True)
            if b < NSEQ:
                add_gates(b, 2)
            if b + 1 < NSEQ:
                for t in range(GT):
                    add(lambda t=t: make_delta(b + 1, 0, t), MM_COST, after_all=(t == 0))
            return cost[0]

        load_x(0)
        add_tasks(-1)
        prefetch()
        for dst, src in ((conv_w[:, :, :], ins["conv_w"]), (conv_b[:, :], ins["conv_b"]), (a_sb[:, :, :], ins["A"]),
                         (dt_bias[:, :], ins["dt_bias"]), (d_param[:, :], ins["D_param"]), (wdt[:, :], ins["w_dt"]),
                         (dt_ln_w[0:R, :], ins["dt_ln_w"]), (dt_ln_w[R:P, :], ins["dt_ln_w"]),
                         (b_ln_w[:, :], ins["b_ln_w"]), (c_ln_w[:, :], ins["c_ln_w"].partition_broadcast(P)),
                         (ffn_b[:, :], ins["ffn_b"]), (gate_b[:, :], ins["gate_b"].partition_broadcast(P)),
                         (lora_b[:, :], ins["lora_b"])):
            consts = sp.dma(lambda e, dst=dst, src=src: e.dma_start(dst, src), const_loaded)
        for lane in (pe, act, dve, pool):
            lane.wait(consts)
        zeroed = pool.op(lambda e: e.memset(identity[:, :], 0.0))
        identity_made = pool.op(lambda e: e.affine_select(
            out=identity[:, :], in_=identity[:, :], compare_op=ALU.not_equal, fill=1.0, base=0,
            pattern=[[-1, P]], channel_multiplier=1), zeroed)
        pe.wait(identity_made)
        halved = dve.op(lambda e: e.tensor_scalar(conv_b[:, :], conv_b[:, :], 0.5, None, ALU.mult), consts)
        taps_halved = dve.op(lambda e: e.tensor_scalar(conv_w[:, :, :], conv_w[:, :, :], 0.5, None, ALU.mult), consts)
        background.drain(HT * MM_COST)

        fetch_b(units[0])
        make_du(0, 0)
        fetch_b(units[1])
        make_drive(units[0])
        for t in range(GT):
            make_decay(units[0], t)
        for s, unit in enumerate(units):
            b, g, n = unit
            if g == 0 and n == 0:
                pace = add_tasks(b) / (NG * N - 3)
                prefetch()
            after = units[s + 1] if s + 1 < len(units) else None
            if g == NG - 1 and n == N - 1:
                background.drain(HT * MM_COST)
            if s:
                turn_state(units[s - 1])
            if after is not None:
                if after[2] == 0:
                    make_du(after[0], after[1])
                make_drive(after)
                if s + 2 < len(units) and units[s + 2][0] in phase:
                    fetch_b(units[s + 2])
            for t in range(GT):
                scan(unit, t)
                if after is not None:
                    make_decay(after, t)
            background.run(pace / 2)
            if s:
                for tt in range(TT):
                    add_y(units[s - 1], tt)
                if n == 0:
                    turn_y(*units[s - 1][0:2])
            background.step_tails()
            background.run(pace / 2)
            if g + 1 < NG and n in (2, 4, 6, 8):
                background.add_beside(make_delta(b, g + 1, n // 2 - 1))
            background.step_tails()
        turn_state(units[-1])
        for tt in range(TT):
            add_y(units[-1], tt)
        turn_y(*units[-1][0:2])
        add_tasks(NSEQ)
        prefetch()
        background.drain(HT * MM_COST)
        sp.wait((out_stored.semaphore, out_stored.count), (b_stored.semaphore, b_stored.count))

        block = ctx.enter_context(nc.Block())

        @block.sync
        def _(engine):
            sp.play(engine)

        @block.tensor
        def _(engine):
            pe.play(engine)

        @block.vector
        def _(engine):
            dve.play(engine)

        @block.scalar
        def _(engine):
            act.play(engine)

        @block.gpsimd
        def _(engine):
            pool.play(engine)


def kernel(**inputs):
    import numpy as np
    import concourse.bacc as bacc
    from concourse.bass_utils import run_bass_kernel_spmd

    P = 128
    g = {k: np.asarray(v) for k, v in inputs.items()}
    x = g["L0_attn_hidden_states"]
    nseq, T, H = x.shape
    D = g["L0_attn_W_out"].shape[1]
    R = g["L0_attn_dt_ln_w"].shape[0]

    def lhs_tiles(w):
        m, k = w.shape
        return w.reshape(m // P, P, k // P, P).transpose(0, 3, 2, 1)

    def by_partition(v):
        return np.moveaxis(v.reshape(-1, P, *v.shape[1:]), 0, 1)

    def on_halves(w):
        return np.concatenate(np.split(w, 2, axis=1), axis=0)

    w_out = lhs_tiles(g["L0_attn_W_out"])
    arrays = {
        "x_rows": x,
        "x_cols": x.transpose(0, 2, 1).reshape(nseq, H // P, P, T).transpose(0, 2, 1, 3),
        "w_in": lhs_tiles(g["L0_attn_W_in"]),
        "w_out": w_out.reshape(H // P, P, 2, D // P // 2, P).transpose(0, 2, 1, 3, 4),
        "w_ffn": lhs_tiles(g["L0_ffn_W"]),
        "w_x": by_partition(g["L0_attn_Wx"].T),
        "w_dt": on_halves(g["L0_attn_Wdt"].T),
        "lora_a": by_partition(g["L0_ffn_A"].T),
        "lora_b": on_halves(g["L0_ffn_B"].T),
        "gate_w": by_partition(g["L0_ffn_gate_w"].T),
        "gate_b": g["L0_ffn_gate_b"],
        "ffn_b": by_partition(g["L0_ffn_b"]),
        "conv_w": by_partition(g["L0_attn_conv_w"]),
        "conv_b": by_partition(g["L0_attn_conv_b"]),
        "dt_bias": by_partition(g["L0_attn_dt_bias"]),
        "D_param": by_partition(g["L0_attn_D_param"]),
        "A": by_partition(g["L0_attn_A"]),
        "dt_ln_w": g["L0_attn_dt_ln_w"][:, None],
        "b_ln_w": g["L0_attn_b_ln_w"][:, None],
        "c_ln_w": g["L0_attn_c_ln_w"],
    }
    arrays = {f"in_{k}": np.ascontiguousarray(v) for k, v in arrays.items()}
    nc = bacc.Bacc("TRN2", target_bir_lowering=False, num_devices=1, dynamic_dma_scratch_size=64)
    ins = {k[3:]: nc.dram_tensor(k, v.shape, mybir.dt.from_np(v.dtype), kind="ExternalInput").ap()
           for k, v in arrays.items()}
    out = nc.dram_tensor("out", x.shape, F32, kind="ExternalOutput").ap()
    build_mixer_ffn(nc, ins, out)
    result = run_bass_kernel_spmd(nc, [arrays], core_ids=[0])
    return result.results[0]["out"]
```

```python
from contextlib import ExitStack

import concourse.bass as bass
from concourse import mybir

F32 = mybir.dt.float32
F32R = mybir.dt.float32r
ALU = mybir.AluOpType
ACT = mybir.ActivationFunctionType
AX = mybir.AxisListType

P = 128
MIXER_EPS = 1e-6
LN_EPS = 1e-5
LORA_RANKS = (8, 16, 32, 64)
SOFTPLUS_CAP = 30.0


class Lane:

    def __init__(self, semaphore):
        self.semaphore, self.count, self.queue = semaphore, 0, []

    def op(self, build, *waits, signal=True):
        self.queue.append((build, [w for w in waits if w is not None], self.semaphore if signal else None, 1))
        self.count += signal
        return (self.semaphore, self.count)

    def dma(self, build, done, *waits):
        self.queue.append((build, [w for w in waits if w is not None], done.semaphore, 16))
        done.count += 16
        return (done.semaphore, done.count)

    def wait(self, *waits):
        self.queue.append((None, list(waits), None, 0))

    def play(self, engine):
        reached = {}
        for build, waits, semaphore, step in self.queue:
            for sem, value in waits:
                if reached.get(id(sem), 0) < value:
                    engine.wait_ge(sem, value)
                    reached[id(sem)] = value
            if build is not None:
                ins = build(engine)
                if semaphore is not None:
                    ins.then_inc(semaphore, step)


class DmaCounter:
    def __init__(self, semaphore):
        self.semaphore, self.count = semaphore, 0


class Ring:

    def __init__(self, buffers, settle=None):
        self.buffers, self.next, self.settle = buffers, 0, settle
        self.free = [()] * len(buffers)

    def take(self):
        i = self.next % len(self.buffers)
        self.next += 1
        while self.free[i] is None:
            self.settle()
        marks, self.free[i] = self.free[i], None
        return i, self.buffers[i], marks

    def open(self):
        return self.free[self.next % len(self.buffers)] is not None

    def release(self, i, *marks):
        self.free[i] = marks


TAIL = "tail"


class Background:

    def __init__(self):
        self.tasks, self.head, self.tails, self.owed = [], None, [], 0.0

    def add(self, task, after_all=False):
        self.tasks.append((task, after_all))

    def run(self, amount):
        self.owed += amount
        while self.owed > 0 and (self.head is not None or self.tasks):
            if self.head is None:
                task, after_all = self.tasks.pop(0)
                while after_all and self.tails:
                    self.step_tails()
                self.head = task()
            self.run_head()
        if self.head is None and not self.tasks:
            self.owed = 0.0

    def run_head(self):
        try:
            cost = next(self.head)
        except StopIteration:
            self.head = None
            return
        if cost is TAIL:
            self.tails.append(self.head)
            self.head = None
        else:
            self.owed -= cost

    def add_beside(self, task):
        while next(task) is not TAIL:
            pass
        self.tails.append(task)

    def step_tails(self):
        for tail in list(self.tails):
            if not tail.gi_running and next(tail, None) is None and tail in self.tails:
                self.tails.remove(tail)

    def settle(self):
        self.step_tails()
        if self.head is not None and not self.head.gi_running:
            self.run_head()

    def drain(self, step, between):
        while self.head is not None or self.tasks or self.tails:
            self.run(step)
            self.step_tails()
            between()


def build_mixer_ffn(nc, ins, out):
    x_rows, x_cols = ins["x_rows"], ins["x_cols"]
    NSEQ, T, H = x_rows.shape
    N = ins["A"].shape[2]
    R = ins["dt_ln_w"].shape[0]
    D = ins["A"].shape[1] * P
    TT, HT, DT = T // P, H // P, D // P
    GT = 4
    NG = DT // GT
    S = R + 2 * N
    KC = ins["conv_w"].shape[2]
    NR = len(LORA_RANKS)
    RMAX = LORA_RANKS[-1]
    WK = 4
    assert T == WK * P and H % T == 0 and R == RMAX == 64 and 2 * R == P and D == 2 * H

    with ExitStack() as ctx:
        def sbuf(name, shape, dtype=F32):
            return ctx.enter_context(nc.sbuf_tensor(name, shape, dtype))

        def psum(name, shape):
            return ctx.enter_context(nc.psum_tensor(name, shape, F32))

        def sem(name):
            return ctx.enter_context(nc.semaphore(name))

        b_rows_dram = nc.dram_tensor("b_rows", [NSEQ, N, T], F32, kind="Internal").ap()
        split_dram = nc.dram_tensor("w_split", [2 * DT + HT, HT // WK, P, 2, WK * P], F32, kind="Internal").ap()
        gates_dram = nc.dram_tensor("gates", [NSEQ, DT, P, T], F32, kind="Internal").ap()

        background = Background()
        settle = background.settle

        rows = sbuf("rows", [P, TT, H])
        cols_high = sbuf("cols_high", [P, HT, T], F32R)
        cols_low = sbuf("cols_low", [P, HT, T], F32R)
        raw_slots = Ring([sbuf(f"w_raw{i}", [P, WK * P]) for i in range(4)])
        split_slots = Ring([sbuf(f"w_split{i}", [P, 2, WK * P], F32R) for i in range(4)])
        chan = [sbuf(f"channels{i}", [P, DT, T]) for i in range(2)]
        delta = sbuf("delta", [P, 2, GT, T])
        du = sbuf("delta_u", [P, GT, T])
        b_bcast = Ring([sbuf(f"b_bcast{i}", [P, T]) for i in range(2)])
        drive = Ring([sbuf(f"drive{i}", [P, GT, T]) for i in range(2)])
        decay = Ring([sbuf(f"decay{i}", [P, T]) for i in range(4)])
        y_acc = sbuf("y_acc", [P, TT, GT * P])
        scratch = Ring([sbuf(f"scratch{i}", [P, T]) for i in range(5)], settle)
        identity = sbuf("identity", [P, P])
        a_sb = sbuf("a_sb", [P, DT, N])
        conv_w = sbuf("conv_w_sb", [P, DT, KC])
        conv_b = sbuf("conv_b_sb", [P, DT])
        dt_bias = sbuf("dt_bias_sb", [P, DT])
        d_param = sbuf("d_param_sb", [P, DT])
        wdt = sbuf("wdt_sb", [P, DT // 2 * P])
        dt_ln_w = sbuf("dt_ln_w_sb", [P, 1])
        b_ln_w = sbuf("b_ln_w_sb", [N, 1])
        c_ln_w = sbuf("c_ln_w_sb", [P, N])
        ffn_b = sbuf("ffn_b_sb", [P, HT])
        gate_b = sbuf("gate_b_sb", [P, NR])
        lora_b = sbuf("lora_b_sb", [P, HT // 2 * P])
        narrow = sbuf("narrow", [P, TT, S])
        ssm_rstd = sbuf("ssm_rstd", [P, 3, TT])
        twice_rows = sbuf("twice_rows", [P, TT, 2 * R])
        c_rows = [sbuf(f"c_rows{i}", [P, TT, N]) for i in range(2)]
        dt_cols = sbuf("dt_cols", [P, T])
        lora_cols = sbuf("lora_cols", [P, T])
        ln_stats = sbuf("ln_stats", [P, TT, H // 512, 6])
        ln_mv = sbuf("ln_mv", [P, TT, 2])
        ln_rstd = sbuf("ln_rstd", [P, TT])
        score = sbuf("score", [P, TT, NR])
        prob = sbuf("prob", [P, TT, NR])
        keep = sbuf("keep", [P, TT, NR])
        row_stat = sbuf("row_stat", [P, 2, TT])

        banks = Ring([psum(f"bank{i}", [P, T]) for i in range(4)], settle)
        state_banks = [psum(f"state_t{i}", [P, GT * P]) for i in range(TT)]

        pe, dve, act, pool, sp = (Lane(sem(n)) for n in
                                  ("tensor_done", "vector_done", "scalar_done", "pool_done", "sync_done"))
        const_loaded = DmaCounter(sem("const_loaded"))
        raw_loaded = [DmaCounter(sem(f"raw_loaded{i}")) for i in range(len(raw_slots.buffers))]
        split_loaded = [DmaCounter(sem(f"split_loaded{i}")) for i in range(len(split_slots.buffers))]
        split_stored = [DmaCounter(sem(f"split_stored{i}")) for i in range(len(split_slots.buffers))]
        rows_loaded = DmaCounter(sem("rows_loaded"))
        b_loaded = [DmaCounter(sem(f"b_loaded{i}")) for i in range(len(b_bcast.buffers))]
        b_stored = DmaCounter(sem("b_stored"))
        gate_stored = [DmaCounter(sem(f"gate_stored{i}")) for i in range(DT)]
        gate_loaded = [DmaCounter(sem(f"gate_loaded{i}")) for i in range(len(scratch.buffers))]
        out_stored = DmaCounter(sem("out_stored"))

        RAW, SPLIT, X, PAIR = range(4)
        raw_plan, pair_plan, to_split, raw_ready, split_ready, to_store = [], [], [], [], [], []
        seen = set()
        planned, placed = [0], [0]
        split_in_dram = {}
        x_open = set()
        cols_free = [()]
        x_ready = {}

        def halves(slot):
            return [slot[:, half, :].rearrange("p (k m) -> p k m", k=WK) for half in range(2)]

        def split_next():
            if not to_split:
                return False
            kind, i, slot, loaded, where = to_split[0]
            if kind == SPLIT and where[0] == placed[0] and split_slots.open():
                si, pair, free = split_slots.take()
                high, low = pair[:, 0, :], pair[:, 1, :]
            elif kind == X and where[0] in x_open:
                high, low, free = cols_high[:, where[1], :], cols_low[:, where[1], :], cols_free[0]
            else:
                return False
            to_split.pop(0)
            rounded = act.op(lambda e: e.activation(high, slot[:, :], ACT.Copy), loaded, *free)
            engine = dve if kind == X and where[0] == 0 else pool
            rest = engine.op(lambda e: e.tensor_tensor(low, slot[:, :], high.bitcast(F32), ALU.subtract), rounded, *free)
            raw_slots.release(i, rest)
            if kind == SPLIT:
                placed[0] += 1
                split_ready.append((si, *halves(pair), rest))
                to_store.append((si, pair, rest, where[1]))
            else:
                x_ready[where] = rest
            return True

        def store_splits():
            while to_store:
                si, pair, made, key = to_store.pop(0)
                split_in_dram[key] = sp.dma(lambda e, pair=pair, key=key: e.dma_start(split_dram[key], pair[:, :, :].bitcast(F32)),
                                            split_stored[si], made)

        def load_free_slots():
            while raw_plan and raw_slots.open():
                kind, parts, cols, where = raw_plan.pop(0)
                i, slot, free = raw_slots.take()
                tile = slot[:, 0:WK * cols].rearrange("p (k m) -> p k m", k=WK)
                for a, z, src in parts:
                    mark = sp.dma(lambda e, dst=tile[:, :, a:z], src=src: e.dma_start(dst, src), raw_loaded[i], *free)
                (raw_ready if kind == RAW else to_split).append((kind, i, tile if kind == RAW else slot, mark, where))
            while pair_plan and pair_plan[0][0] == placed[0] and split_slots.open():
                _, key = pair_plan.pop(0)
                placed[0] += 1
                si, pair, free = split_slots.take()
                loaded = sp.dma(lambda e, pair=pair, key=key: e.dma_start(pair[:, :, :].bitcast(F32), split_dram[key]),
                                split_loaded[si], split_in_dram[key], *free)
                split_ready.append((si, *halves(pair), loaded))

        def stream():
            store_splits()
            for _ in range(len(to_split)):
                if not split_next():
                    break
            load_free_slots()

        def next_of(ready):
            while not ready:
                stream()
            return ready.pop(0)

        def plan_raw(src, n_k):
            for k in range(0, n_k, WK):
                raw_plan.append((RAW, [(0, P, src[:, k:k + WK, :])], P, None))

        def plan_split(tile, src):
            for half in range(HT // WK):
                key = tile, half
                if key in seen:
                    pair_plan.append((planned[0], key))
                else:
                    seen.add(key)
                    raw_plan.append((SPLIT, [(0, P, src[:, half * WK:(half + 1) * WK, :])], P, (planned[0], key)))
                planned[0] += 1
        def plan_x(b):
            for k in range(HT):
                src = x_cols[b][:, k, :].rearrange("p (a q) -> p a q", a=WK)
                raw_plan.append((X, [(0, P, src)], P, (b, k)))

        def open_x(b):
            x_open.add(b)
            stream()

        MM_COST = 0.86
        MM3_COST = 0.65
        TURN_COST = 0.11

        def product(moving, n_k, *waits):
            bi, bank, free = banks.take()
            for k in range(n_k):
                if k % WK == 0:
                    _, w_i, w, loaded, _ = next_of(raw_ready)
                end_of_slot = k % WK == WK - 1
                mark = pe.op(lambda e, w=w, k=k: e.matmul(
                    bank[:, :], w[:, k % WK, :], moving(k), start=(k == 0), stop=(k == n_k - 1)),
                    loaded, *(free + waits if k == 0 else ()), signal=end_of_slot)
                if end_of_slot:
                    raw_slots.release(w_i, mark)
                    yield WK * MM_COST
            return bi, bank, mark

        def split_product(ready, extra=None):
            bi, bank, free = banks.take()
            for k in range(HT):
                if k % WK == 0:
                    w_i, high, low, loaded = next_of(split_ready)
                    store_splits()
                while ready(k) is None:
                    stream()
                terms = ((high, cols_high), (high, cols_low), (low, cols_high))
                for n, (w, x) in enumerate(terms):
                    end_of_slot = k % WK == WK - 1 and n == 2
                    mark = pe.op(lambda e, w=w, x=x, k=k, first=(k == 0 and n == 0),
                                 last=(k == HT - 1 and n == 2 and extra is None): e.matmul(
                        bank[:, :], w[:, k % WK, :], x[:, k, :], start=first, stop=last),
                        loaded, ready(k), *(free if k == 0 else ()), signal=end_of_slot)
                if end_of_slot:
                    split_slots.release(w_i, mark, (split_stored[w_i].semaphore, split_stored[w_i].count))
                    load_free_slots()
                    yield WK * MM3_COST
            cols_free[0] = (mark,)
            if extra is not None:
                lhsT, rhs, extra_mark = extra()
                mark = pe.op(lambda e: e.matmul(bank[:, :], lhsT, rhs, start=False, stop=True), consts, extra_mark)
                yield MM_COST
            return bi, bank, mark

        def turn(bank, tiles, *waits):
            for i, tile in enumerate(tiles):
                mark = pe.op(lambda e, i=i, tile=tile: e.transpose(
                    bank[0:tile.shape[1], i * P:(i + 1) * P], tile, identity[:, :]), identity_made, *waits,
                    signal=(i == len(tiles) - 1))
            return mark

        u_ready = {}
        chan_free = [(), ()]

        def make_u(b, j):
            bi, bank, mark = yield from split_product(lambda k: x_ready.get((b, k)))
            yield TAIL
            ci, conv, conv_free = scratch.take()
            ti, th, th_free = scratch.take()
            done = act.op(lambda e: e.activation(conv[:, :], bank[:, :], ACT.Identity, bias=conv_b[:, j:j + 1],
                                                 scale=conv_w[:, j, KC - 1:KC]), mark, consts, taps_halved, *conv_free)
            yield 0
            for back in range(1, KC):
                done = dve.op(lambda e, back=back: e.scalar_tensor_tensor(
                    conv[:, back:T], bank[:, 0:T - back], conv_w[:, j, KC - 1 - back:KC - back],
                    conv[:, back:T], ALU.mult, ALU.add), done, mark)
            banks.release(bi, done)
            yield 0
            tanh = act.op(lambda e: e.activation(th[:, :], conv[:, :], ACT.Tanh), done, *th_free)
            yield 0
            u = chan[b % 2][:, j, :]
            made = dve.op(lambda e: e.scalar_tensor_tensor(u, th[:, :], 1.0, conv[:, :], ALU.add, ALU.mult),
                          tanh, *chan_free[b % 2])
            scratch.release(ci, made)
            scratch.release(ti, made)
            u_ready[b, j] = made

        phase = {}
        free_after = dict(c_rows=[(), ()], narrow=(), twice_rows=(), dt_cols=(), lora_cols=(), du=(), ln=())

        def plan_ssm():
            for k in range(0, DT, WK):
                raw_plan.append((RAW, [(0, S, ins["w_x"][:, k:k + WK, :])], S, None))

        def make_ssm(b):
            u = chan[b % 2]
            weights = [next_of(raw_ready) for _ in range(DT // WK)]
            si, bank, free = banks.take()
            rows = bank[:, 0:TT * S].rearrange("p (a s) -> p a s", a=TT)
            for tt in range(TT):
                for k in range(DT):
                    _, _, w, loaded, _ = weights[k // WK]
                    mark = pe.op(lambda e, tt=tt, k=k, w=w: e.matmul(
                        rows[:, tt, :], u[:, k, tt * P:(tt + 1) * P], w[:, k % WK, :],
                        start=(k == 0), stop=(k == DT - 1)), loaded, u_ready[b, k], *free,
                        signal=(k == DT - 1))
                yield DT * 0.17
            for _, w_i, _, _, _ in weights:
                raw_slots.release(w_i, mark)
            yield TAIL
            copied = act.op(lambda e: e.activation(narrow[:, :, :], rows, ACT.Copy), mark, *free_after["narrow"])
            banks.release(si, copied)
            yield 0
            squares = twice_rows[:, :, 0:S]
            squared = dve.op(lambda e: e.tensor_tensor(squares, narrow[:, :, :], narrow[:, :, :], ALU.mult),
                             copied, *free_after["twice_rows"])
            segments = ((0, R), (R, R + N), (R + N, S))
            for i, (a, z) in enumerate(segments):
                summed = dve.op(lambda e, i=i, a=a, z=z: e.tensor_reduce(
                    ssm_rstd[:, i, :], squares[:, :, a:z], AX.X, ALU.add), squared)
            free_after["twice_rows"] = (summed,)
            for i, (a, z) in enumerate(segments):
                means = dve.op(lambda e, i=i, a=a, z=z: e.tensor_scalar(
                    ssm_rstd[:, i, :], ssm_rstd[:, i, :], 1.0 / (z - a), MIXER_EPS, ALU.mult, ALU.add), summed)
            rooted = act.op(lambda e: e.activation(ssm_rstd[:, :, :], ssm_rstd[:, :, :], ACT.Sqrt), means)
            yield 0
            rstd = dve.op(lambda e: e.reciprocal(ssm_rstd[:, :, :], ssm_rstd[:, :, :]), rooted)
            c = c_rows[b % 2]
            for tt in range(TT):
                for half in range(2):
                    dt_done = dve.op(lambda e, tt=tt, half=half: e.tensor_scalar(
                        twice_rows[:, tt, half * R:(half + 1) * R], narrow[:, tt, 0:R], ssm_rstd[:, 0, tt:tt + 1], None,
                        ALU.mult), rstd, *free_after["twice_rows"])
                b_done = dve.op(lambda e, tt=tt: e.tensor_scalar(
                    narrow[:, tt, R:R + N], narrow[:, tt, R:R + N], ssm_rstd[:, 1, tt:tt + 1], None, ALU.mult), rstd)
                c_done = dve.op(lambda e, tt=tt: e.scalar_tensor_tensor(
                    c[:, tt, :], narrow[:, tt, R + N:S], ssm_rstd[:, 2, tt:tt + 1], c_ln_w[:, :], ALU.mult, ALU.mult),
                    rstd, *free_after["c_rows"][b % 2])
            yield 0
            si, bank, free = banks.take()
            mark = turn(bank, [twice_rows[:, tt, :] for tt in range(TT)], dt_done, *free)
            free_after["twice_rows"] = (mark,)
            dt_mark = act.op(lambda e, bank=bank: e.activation(dt_cols[:, :], bank[:, :], ACT.Copy, scale=dt_ln_w[:, :]),
                             mark, *free_after["dt_cols"])
            banks.release(si, dt_mark)
            si, bank, free = banks.take()
            mark = turn(bank, [narrow[:, tt, R:R + N] for tt in range(TT)], b_done, *free)
            free_after["narrow"] = (mark, c_done)
            ci, b_cols, free = scratch.take()
            b_mark = act.op(lambda e, bank=bank: e.activation(b_cols[0:N, :], bank[0:N, :], ACT.Copy, scale=b_ln_w[:, :]),
                            mark, *free)
            banks.release(si, b_mark)
            stored = sp.dma(lambda e: e.dma_start(b_rows_dram[b, :, :], b_cols[0:N, :]), b_stored, b_mark)
            scratch.release(ci, stored)
            phase[b] = dict(dt=dt_mark, b=stored, c=c_done)

        delta_free = {}
        delta_ready, du_ready = {}, {}

        def make_delta(b, g, t):
            j = g * GT + t
            half, col = j // (DT // 2), j % (DT // 2) * P
            dst = delta[:, g % 2, t, :]
            si, bank, free = banks.take()
            mark = pe.op(lambda e: e.matmul(
                bank[:, :], wdt[half * R:(half + 1) * R, col:col + P], dt_cols[half * R:(half + 1) * R, :],
                start=True, stop=True), phase[b]["dt"], consts, *free)
            free_after["dt_cols"] = (mark,)
            yield MM_COST
            yield TAIL
            v = act.op(lambda e: e.activation(dst, bank[:, :], ACT.Identity, bias=dt_bias[:, j:j + 1]),
                       mark, *delta_free.get((g % 2, t), ()))
            banks.release(si, v)
            ei, ex, ex_free = scratch.take()
            capped = dve.op(lambda e: e.tensor_scalar(ex[:, :], dst, SOFTPLUS_CAP, None, ALU.min), v, *ex_free)
            yield 0
            exped = act.op(lambda e: e.activation(ex[:, :], ex[:, :], ACT.Exp), capped)
            logged = act.op(lambda e: e.activation(ex[:, :], ex[:, :], ACT.Ln, bias=1.0), exped)
            yield 0
            yield 0
            made = dve.op(lambda e: e.tensor_tensor(dst, dst, ex[:, :], ALU.max), logged)
            scratch.release(ei, made)
            delta_ready[b, g, t] = made

        def make_du(b, g):
            marks = []
            for t in range(GT):
                j = g * GT + t
                marks.append((pool if t < GT // 2 else dve).op(lambda e, t=t, j=j: e.tensor_tensor(
                    du[:, t, :], delta[:, g % 2, t, :], chan[b % 2][:, j, :], ALU.mult),
                    delta_ready[b, g, t], u_ready[b, j], *free_after["du"]))
            du_ready[b, g] = (marks[GT // 2 - 1], marks[-1])

        y_ready = {}
        y_acc_free = [()]

        def turn_y(b, g):
            for t in range(GT):
                j = g * GT + t
                si, bank, free = banks.take()
                mark = turn(bank, [y_acc[:, tt, t * P:(t + 1) * P] for tt in range(TT)], *last_add, *free)
                u = chan[b % 2][:, j, :]
                y_ready[b, j] = dve.op(lambda e, bank=bank, u=u, j=j: e.scalar_tensor_tensor(
                    u, u, d_param[:, j:j + 1], bank[:, :], ALU.mult, ALU.add), mark, *du_ready[b, g])
                banks.release(si, y_ready[b, j])
                background.add_beside(gate_y(b, j))
            y_acc_free[0] = (mark,)

        def make_gate(b, j):
            bi, bank, mark = yield from split_product(lambda k: x_ready.get((b, k)))
            yield TAIL
            gi, gate, free = scratch.take()
            tanh = act.op(lambda e: e.activation(gate[:, :], bank[:, :], ACT.Tanh, scale=0.5), mark, *free)
            yield 0
            twice = dve.op(lambda e: e.scalar_tensor_tensor(
                gate[:, :], gate[:, :], 1.0, bank[:, :], ALU.add, ALU.mult), tanh)
            banks.release(bi, twice)
            yield 0
            gate_in_dram[b, j] = sp.dma(lambda e: e.dma_start(gates_dram[b, j], gate[:, :]), gate_stored[j], twice)
            scratch.release(gi, gate_in_dram[b, j])

        gate_in_dram = {}

        def gate_y(b, j):
            yield TAIL
            yield 0
            yield 0
            gi, gate, free = scratch.take()
            loaded = sp.dma(lambda e: e.dma_start(gate[:, :], gates_dram[b, j]), gate_loaded[gi],
                            gate_in_dram[b, j], *free)
            yield 0
            y = chan[b % 2][:, j, :]
            y_ready[b, j] = dve.op(lambda e: e.scalar_tensor_tensor(
                y, y, 0.5, gate[:, :], ALU.mult, ALU.mult), loaded, y_ready[b, j])
            scratch.release(gi, y_ready[b, j])

        mixed = {}

        rows_free = [()]

        def load_rows(b):
            mixed["rows"] = sp.dma(lambda e: e.dma_start(rows[:, :, :], x_rows[b].rearrange("(a p) h -> p a h", p=P)),
                                   rows_loaded, *rows_free[0])

        def add_to_rows(h, bi, bank, mark, bias):
            ci, cols, free = scratch.take()
            copied = act.op(lambda e: e.activation(cols[:, :], bank[:, :], ACT.Identity, bias=bias), mark, *free)
            banks.release(bi, copied)
            yield 0
            si, side, free = banks.take()
            turned = turn(side, [cols[:, tt * P:(tt + 1) * P] for tt in range(TT)], copied, *free)
            scratch.release(ci, turned)
            yield 0
            dst = rows[:, :, h * P:(h + 1) * P]
            added = dve.op(lambda e: e.tensor_tensor(dst, side[:, :].rearrange("p (a q) -> p a q", a=TT), dst, ALU.add),
                           turned, mixed["rows"])
            banks.release(si, added)
            mixed["added"] = added

        def make_out(b, h):
            y = chan[b % 2]
            info = yield from product(lambda k: y[:, k, :], DT, *[y_ready[b, j] for j in range(DT)])
            chan_free[b % 2] = (info[2],)
            yield TAIL
            yield from add_to_rows(h, *info, 0.0)

        def layer_norm():
            yield TAIL
            for tt in range(TT):
                for i in range(H // 512):
                    stats = dve.op(lambda e, tt=tt, i=i: e.bn_stats(
                        ln_stats[:, tt, i, :], rows[:, tt, i * 512:(i + 1) * 512]), mixed["added"], *free_after["ln"])
                aggr = dve.op(lambda e, tt=tt: e.bn_aggr(ln_mv[:, tt, :], ln_stats[:, tt, :, :]), stats)
                yield 0
            added = dve.op(lambda e: e.tensor_scalar(ln_rstd[:, :], ln_mv[:, :, 1], LN_EPS, None, ALU.add), aggr)
            rooted = act.op(lambda e: e.activation(ln_rstd[:, :], ln_rstd[:, :], ACT.Sqrt), added)
            yield 0
            rstd = dve.op(lambda e: e.reciprocal(ln_rstd[:, :], ln_rstd[:, :]), rooted)
            mixed["normed"] = []
            for tt in range(TT):
                mixed["normed"].append(dve.op(lambda e, tt=tt: e.tensor_scalar(
                    rows[:, tt, :], rows[:, tt, :], ln_mv[:, tt, 0:1], ln_rstd[:, tt:tt + 1],
                    ALU.subtract, ALU.mult), rstd))
                if tt % 2:
                    yield 0
            free_after["ln"] = (mixed["normed"][-1],)

        def x1_by_columns():
            before = cols_free[0]
            for h in range(HT):
                si, bank, free = banks.take()
                mark = turn(bank, [rows[:, tt, h * P:(h + 1) * P] for tt in range(TT)], *mixed["normed"], *free)
                high, low = cols_high[:, h, :], cols_low[:, h, :]
                rounded = act.op(lambda e, high=high, bank=bank: e.activation(high, bank[:, :], ACT.Copy),
                                 mark, *before)
                mixed["x1"] = dve.op(lambda e, high=high, low=low, bank=bank: e.tensor_tensor(
                    low, bank[:, :], high.bitcast(F32), ALU.subtract), rounded)
                banks.release(si, mixed["x1"])
                yield TT * TURN_COST
            mixed["rows"] = mark

        def plan_route():
            for k in range(0, HT, WK):
                raw_plan.append((RAW, [(0, RMAX, ins["lora_a"][:, k:k + WK, :]),
                                          (RMAX, RMAX + NR, ins["gate_w"][:, k:k + WK, :])], RMAX + NR, None))

        def route():
            weights = [next_of(raw_ready) for _ in range(HT // WK)]
            si, bank, free = banks.take()
            C = RMAX + NR
            both = bank[:, 0:TT * C].rearrange("p (a c) -> p a c", a=TT)
            for tt in range(TT):
                for part, x1 in enumerate((cols_high, cols_low)):
                    for k in range(HT):
                        _, _, w, loaded, _ = weights[k // WK]
                        last = part == 1 and k == HT - 1
                        mark = pe.op(lambda e, tt=tt, k=k, w=w, x1=x1, part=part, last=last: e.matmul(
                            both[:, tt, :], x1[:, k, tt * P:(tt + 1) * P].bitcast(F32), w[:, k % WK, :],
                            start=(k == 0 and part == 0), stop=last), loaded, mixed["x1"], *free, signal=last)
                yield 2.0
            cols_free[0] = (mark,)
            for _, w_i, _, _, _ in weights:
                raw_slots.release(w_i, mark)
            lora_raw = narrow[:, :, 0:C]
            copied = act.op(lambda e: e.activation(lora_raw, both, ACT.Copy), mark, *free_after["narrow"])
            banks.release(si, copied)
            mixed.pop("lora", None)
            yield TAIL

            def per_token(ap):
                return ap.unsqueeze(2).broadcast_to([P, TT, NR])
            gate_bias = gate_b[:, :].unsqueeze(1).broadcast_to([P, TT, NR])
            top, total = row_stat[:, 0, :], row_stat[:, 1, :]
            c = dve.op(lambda e: e.tensor_tensor(score[:, :, :], narrow[:, :, RMAX:C], gate_bias, ALU.add),
                       copied, *free_after["twice_rows"])
            c = dve.op(lambda e: e.tensor_reduce(top, score[:, :, :], AX.X, ALU.max), c)
            c = dve.op(lambda e: e.tensor_tensor(score[:, :, :], score[:, :, :], per_token(top), ALU.subtract), c)
            exped = act.op(lambda e: e.activation(prob[:, :, :], score[:, :, :], ACT.Exp), c)
            yield 0
            c = dve.op(lambda e: e.tensor_reduce(total, prob[:, :, :], AX.X, ALU.add), exped)
            c = dve.op(lambda e: e.reciprocal(total, total), c)
            c = dve.op(lambda e: e.tensor_tensor(prob[:, :, :], prob[:, :, :], per_token(total), ALU.mult), c)
            c = dve.op(lambda e: e.tensor_reduce(top, prob[:, :, :], AX.X, ALU.max), c)
            c = dve.op(lambda e: e.reciprocal(total, top), c)
            c = dve.op(lambda e: e.tensor_tensor(keep[:, :, 0], top, total, ALU.mult), c)
            c = dve.op(lambda e: e.tensor_tensor(score[:, :, :], prob[:, :, :], per_token(top), ALU.is_lt), c)
            for r in range(1, NR):
                c = dve.op(lambda e, r=r: e.tensor_tensor(
                    keep[:, :, r], keep[:, :, r - 1], score[:, :, r - 1], ALU.mult), c)
            yield 0
            start = 0
            for r, rank in enumerate(LORA_RANKS):
                for half in range(2):
                    dst = twice_rows[:, :, half * RMAX + start:half * RMAX + rank]
                    weight = keep[:, :, r:r + 1].broadcast_to([P, TT, rank - start])
                    masked = dve.op(lambda e, dst=dst, weight=weight, a=start, z=rank: e.tensor_tensor(
                        dst, narrow[:, :, a:z], weight, ALU.mult), c, *free_after["twice_rows"])
                start = rank
            free_after["narrow"] = (masked,)
            yield 0
            si, bank2, free = banks.take()
            mark = turn(bank2, [twice_rows[:, tt, :] for tt in range(TT)], masked, *free)
            free_after["twice_rows"] = (mark,)
            mixed["lora"] = act.op(lambda e: e.activation(lora_cols[:, :], bank2[:, :], ACT.Copy), mark,
                                   *free_after["lora_cols"])
            banks.release(si, mixed["lora"])

        def make_ffn(h):
            half, col = h // (HT // 2), h % (HT // 2) * P

            def low_rank():
                while "lora" not in mixed:
                    settle()
                return (lora_b[half * RMAX:(half + 1) * RMAX, col:col + P],
                        lora_cols[half * RMAX:(half + 1) * RMAX, :], mixed["lora"])
            info = yield from split_product(lambda k: mixed["x1"], extra=low_rank)
            free_after["lora_cols"] = (info[2],)
            yield TAIL
            yield from add_to_rows(h, *info, ffn_b[:, h:h + 1])

        def store_rows(b):
            rows_free[0] = (sp.dma(lambda e: e.dma_start(out[b].rearrange("(a p) h -> p a h", p=P), rows[:, :, :]),
                                   out_stored, *mixed["normed"]),)

        state_bank_free = [() for _ in range(TT)]
        drive_of, decay_of, turned_of, scanned_of, b_of = {}, {}, {}, {}, {}
        last_add = [None] * TT
        units = [(b, g, n) for b in range(NSEQ) for g in range(NG) for n in range(N)]

        def fetch_b(unit):
            b, g, n = unit
            i, tile, free = b_bcast.take()
            b_of[unit] = (i, tile, act.dma(lambda e: e.dma_start(
                tile[:, :], b_rows_dram[b, n, :].partition_broadcast(P)), b_loaded[i], phase[b]["b"], *free))

        def make_drive(unit):
            b, g, n = unit
            i, tile, loaded = b_of.pop(unit)
            di, dst, free = drive.take()
            row = tile[:, :].unsqueeze(1).broadcast_to([P, GT, T])
            made = pool.op(lambda e: e.tensor_tensor(dst[:, :, :], du[:, :, :], row, ALU.mult),
                           loaded, *du_ready[b, g], *free)
            b_bcast.release(i, made)
            free_after["du"] = (made,)
            drive_of[unit] = (di, dst, made)

        decay_order = [(unit, t) for unit in units for t in range(GT)]

        def make_next_decay():
            if not decay_order:
                return
            unit, t = decay_order.pop(0)
            b, g, n = unit
            j = g * GT + t
            i, dst, free = decay.take()
            made = act.op(lambda e: e.activation(dst[:, :], delta[:, g % 2, t, :], ACT.Exp, scale=a_sb[:, j, n:n + 1]),
                          delta_ready[b, g, t], *free)
            delta_free[g % 2, t] = (made,)
            decay_of[unit, t] = (i, dst, made)

        def scan(unit, t):
            _, state, driven = drive_of[unit]
            i, dec, decayed = decay_of.pop((unit, t))
            done = dve.op(lambda e: e.tensor_tensor_scan(
                state[:, t, :], dec[:, :], state[:, t, :], 0.0, ALU.mult, ALU.add), driven, decayed)
            decay.release(i, done)
            scanned_of[unit, t] = done

        def turn_state(unit):
            di, state, _ = drive_of.pop(unit)
            for tt in range(TT):
                turned_of[unit, tt] = turn(state_banks[tt], [state[:, t, tt * P:(tt + 1) * P] for t in range(GT)],
                                           scanned_of[unit, GT - 1], *state_bank_free[tt])
            drive.release(di, turned_of[unit, TT - 1])

        def add_y(unit, tt):
            b, g, n = unit
            c = c_rows[b % 2][:, tt, n:n + 1]
            mark = turned_of.pop((unit, tt))
            if n == 0:
                done = dve.op(lambda e: e.tensor_scalar(y_acc[:, tt, :], state_banks[tt][:, :], c, None, ALU.mult),
                              mark, phase[b]["c"], *y_acc_free[0])
            else:
                done = dve.op(lambda e: e.scalar_tensor_tensor(
                    y_acc[:, tt, :], state_banks[tt][:, :], c, y_acc[:, tt, :], ALU.mult, ALU.add),
                    mark, last_add[tt])
            last_add[tt] = done
            state_bank_free[tt] = (done,)
            free_after["c_rows"][b % 2] = (done,)

        def add_tasks(b):
            cost = [0.0]

            def add(task, us=0.0, after_all=False):
                background.add(task, after_all)
                cost[0] += us

            def call(function, *args):
                add(lambda: iter([function(*args) or 0]))

            def add_products(make, name, s, tiles, offset=0):
                for j in tiles:
                    plan_split(offset + j, ins[name][offset + j])
                    add(lambda j=j: make(s, j), HT * MM3_COST)

            EARLY = 4
            FIRST = 4
            s = b - 1
            if 0 <= b < NSEQ:
                add_products(make_gate, "w_in", b, range(EARLY, EARLY + FIRST), DT)
            if s >= 0:
                background.add(lambda: iter([load_rows(s) or 0]), after_all=True)
                for h in range(HT):
                    plan_raw(ins["w_out"][h], DT)
                    add(lambda h=h: make_out(s, h), DT * MM_COST)
                add(layer_norm, after_all=True)
            if 0 <= b < NSEQ:
                add_products(make_gate, "w_in", b, range(EARLY + FIRST, DT), DT)
            if s >= 0:
                add(x1_by_columns, 4.0, after_all=True)
                plan_route()
                add(route, 8.0)
                for h in range(HT):
                    plan_split(2 * DT + h, ins["w_ffn"][h])
                    add(lambda h=h: make_ffn(h), HT * MM3_COST + MM_COST)
                add(layer_norm, after_all=True)
            if b + 1 < NSEQ:
                plan_x(b + 1)
                call(open_x, b + 1)
                add_products(make_u, "w_in", b + 1, range(DT))
            if s >= 0:
                background.add(lambda: iter([store_rows(s) or 0]), after_all=True)
            if b + 1 < NSEQ:
                plan_ssm()
                add(lambda: make_ssm(b + 1), 11.0, after_all=True)
                add_products(make_gate, "w_in", b + 1, range(EARLY), DT)
                for t in range(GT):
                    add(lambda t=t: make_delta(b + 1, 0, t), MM_COST, after_all=(t == 0))
            return cost[0]

        add_tasks(-1)
        stream()
        for dst, src in ((conv_w[:, :, :], ins["conv_w"]), (conv_b[:, :], ins["conv_b"]), (a_sb[:, :, :], ins["A"]),
                         (dt_bias[:, :], ins["dt_bias"]), (d_param[:, :], ins["D_param"]), (wdt[:, :], ins["w_dt"]),
                         (dt_ln_w[0:R, :], ins["dt_ln_w"]), (dt_ln_w[R:P, :], ins["dt_ln_w"]),
                         (b_ln_w[:, :], ins["b_ln_w"]), (c_ln_w[:, :], ins["c_ln_w"].partition_broadcast(P)),
                         (ffn_b[:, :], ins["ffn_b"]), (gate_b[:, :], ins["gate_b"].partition_broadcast(P)),
                         (lora_b[:, :], ins["lora_b"])):
            consts = sp.dma(lambda e, dst=dst, src=src: e.dma_start(dst, src), const_loaded)
        zeroed = pool.op(lambda e: e.memset(identity[:, :], 0.0))
        identity_made = pool.op(lambda e: e.affine_select(
            out=identity[:, :], in_=identity[:, :], compare_op=ALU.not_equal, fill=1.0, base=0,
            pattern=[[-1, P]], channel_multiplier=1), zeroed)
        dve.wait(consts)
        halved = dve.op(lambda e: e.tensor_scalar(conv_b[:, :], conv_b[:, :], 0.5, None, ALU.mult), consts)
        taps_halved = dve.op(lambda e: e.tensor_scalar(conv_w[:, :, :], conv_w[:, :, :], 0.5, None, ALU.mult), consts)
        background.drain(HT * MM3_COST, stream)

        pace = add_tasks(0) / (NG * N - 3)
        load_free_slots()
        stream()
        fetch_b(units[0])
        make_du(0, 0)
        fetch_b(units[1])
        make_drive(units[0])
        for _ in decay.buffers:
            make_next_decay()
        for s, unit in enumerate(units):
            b, g, n = unit
            if g == 0 and n == 0 and s:
                pace = add_tasks(b) / (NG * N - 3)
            after = units[s + 1] if s + 1 < len(units) else None
            if g == NG - 1 and n == N - 1:
                background.drain(HT * MM3_COST, stream)
            if s:
                turn_state(units[s - 1])
            if after is not None:
                if after[2] == 0:
                    make_du(after[0], after[1])
                make_drive(after)
                if s + 2 < len(units) and units[s + 2][0] in phase:
                    fetch_b(units[s + 2])
            background.step_tails()
            for t in range(GT):
                scan(unit, t)
                make_next_decay()
            background.step_tails()
            stream()
            if s:
                for tt in range(TT):
                    add_y(units[s - 1], tt)
            if g + 1 < NG and n in (2, 4, 6, 8):
                background.add_beside(make_delta(b, g + 1, n // 2 - 1))
            background.step_tails()
            background.run(pace / 2)
            if s and n == 0:
                turn_y(*units[s - 1][0:2])
            background.run(pace / 2)
        turn_state(units[-1])
        for tt in range(TT):
            add_y(units[-1], tt)
        turn_y(*units[-1][0:2])
        add_tasks(NSEQ)
        background.drain(HT * MM3_COST, stream)
        sp.wait((out_stored.semaphore, out_stored.count), (b_stored.semaphore, b_stored.count),
                *[(c.semaphore, c.count) for c in gate_stored + split_stored])

        block = ctx.enter_context(nc.Block())

        @block.sync
        def _(engine):
            sp.play(engine)

        @block.tensor
        def _(engine):
            pe.play(engine)

        @block.vector
        def _(engine):
            dve.play(engine)

        @block.scalar
        def _(engine):
            act.play(engine)

        @block.gpsimd
        def _(engine):
            pool.play(engine)


def kernel(**inputs):
    import numpy as np
    import concourse.bacc as bacc
    from concourse.bass_utils import run_bass_kernel_spmd

    P = 128
    g = {k: np.asarray(v) for k, v in inputs.items()}
    x = g["L0_attn_hidden_states"]
    nseq, T, H = x.shape
    D = g["L0_attn_W_out"].shape[1]
    R = g["L0_attn_dt_ln_w"].shape[0]

    def lhs_tiles(w):
        m, k = w.shape
        return w.reshape(m // P, P, k // P, P).transpose(0, 3, 2, 1)

    def by_partition(v):
        return np.moveaxis(v.reshape(-1, P, *v.shape[1:]), 0, 1)

    def on_halves(w):
        return np.concatenate(np.split(w, 2, axis=1), axis=0)

    arrays = {
        "x_rows": x,
        "x_cols": x.transpose(0, 2, 1).reshape(nseq, H // P, P, T).transpose(0, 2, 1, 3),
        "w_in": lhs_tiles(g["L0_attn_W_in"]),
        "w_out": lhs_tiles(g["L0_attn_W_out"]),
        "w_ffn": lhs_tiles(g["L0_ffn_W"]),
        "w_x": by_partition(g["L0_attn_Wx"].T),
        "w_dt": on_halves(g["L0_attn_Wdt"].T),
        "lora_a": by_partition(g["L0_ffn_A"].T),
        "lora_b": on_halves(g["L0_ffn_B"].T),
        "gate_w": by_partition(g["L0_ffn_gate_w"].T),
        "gate_b": g["L0_ffn_gate_b"],
        "ffn_b": by_partition(g["L0_ffn_b"]),
        "conv_w": by_partition(g["L0_attn_conv_w"]),
        "conv_b": by_partition(g["L0_attn_conv_b"]),
        "dt_bias": by_partition(g["L0_attn_dt_bias"]),
        "D_param": by_partition(g["L0_attn_D_param"]),
        "A": by_partition(g["L0_attn_A"]),
        "dt_ln_w": g["L0_attn_dt_ln_w"][:, None],
        "b_ln_w": g["L0_attn_b_ln_w"][:, None],
        "c_ln_w": g["L0_attn_c_ln_w"],
    }
    arrays = {f"in_{k}": np.ascontiguousarray(v) for k, v in arrays.items()}
    nc = bacc.Bacc("TRN2", target_bir_lowering=False, num_devices=1, dynamic_dma_scratch_size=64)
    ins = {k[3:]: nc.dram_tensor(k, v.shape, mybir.dt.from_np(v.dtype), kind="ExternalInput").ap()
           for k, v in arrays.items()}
    out = nc.dram_tensor("out", x.shape, F32, kind="ExternalOutput").ap()
    build_mixer_ffn(nc, ins, out)
    result = run_bass_kernel_spmd(nc, [arrays], core_ids=[0])
    return result.results[0]["out"]
```
